# Optimizing a Trainium2 kernel written in Bass

```python
import numpy as np
import jax
import jax.numpy as jnp

def _softmax(x, axis=-1):
    return jax.nn.softmax(x, axis=axis)

def _gelu(x):
    return jax.nn.gelu(x, approximate=True)

def _silu(x):
    return jax.nn.silu(x)

def _sigmoid(x):
    return jax.nn.sigmoid(x)

def _layernorm(x, axis=-1, eps=1e-05):
    m = jnp.mean(x, axis=axis, keepdims=True)
    v = jnp.var(x, axis=axis, keepdims=True)
    return (x - m) / jnp.sqrt(v + eps)

def _scatter_add(tgt, idx, src, axis=0):
    return tgt.at[idx].add(src)

def _segment_sum(src, seg, n):
    return jax.ops.segment_sum(src, seg, n)
kernel_name = 'mk_vit_tower_cls_d1_tok_img1024_r4_459782'

def setup_inputs(seed: int=0):
    np.random.seed(seed)
    _w = jnp.asarray

    def _rec_inputs():
        import jax
        import jax.numpy as jnp
        _rk = jax.random.key(seed)
        x = -0.00016672 + 0.999947 * jax.random.normal(jax.random.fold_in(_rk, 1), (16, 96, 96, 3), jnp.float32)
        cls_tok = 0.02 * jax.random.normal(jax.random.fold_in(_rk, 5), (1, 1, 256), jnp.float32)
        return (x, cls_tok)
    x, cls_tok = _rec_inputs()

    def _L0_tok_setup():
        import jax, jax.numpy as jnp
        import numpy as np
        P = 16
        E = 256

        def patchify(images, patch_size):
            B, H, W, C = images.shape
            hp, wp = (H // patch_size, W // patch_size)
            x = images.reshape(B, hp, patch_size, wp, patch_size, C)
            x = x.transpose(0, 1, 3, 2, 4, 5)
            return x.reshape(B, hp * wp, patch_size * patch_size * C)
        key = jax.random.key(seed)
        k_img, k_w, k_b, k_pos = jax.random.split(key, 4)
        B, H, W, C = (64, 96, 96, 3)
        patch_dim = P * P * C
        patch_count = H // P * (W // P)
        images = jax.random.normal(k_img, (B, H, W, C), dtype=jnp.float32)
        W_proj = jax.random.normal(k_w, (E, patch_dim), dtype=jnp.float32) * patch_dim ** (-0.5)
        b_proj = jax.random.normal(k_b, (E,), dtype=jnp.float32) * 0.02
        pos_emb = jax.random.normal(k_pos, (patch_count, E), dtype=jnp.float32) * 0.02
        return {'images': images, 'W_proj': W_proj, 'b_proj': b_proj, 'pos_emb': pos_emb}
    _L0_tok_all = _L0_tok_setup()
    _L0_tok_in = {k: v for k, v in _L0_tok_all.items() if k in ('W_proj', 'b_proj', 'pos_emb')}
    del _L0_tok_all

    def _L0_attn_setup():
        import jax, jax.numpy as jnp
        import numpy as np
        B, T, C = (2, 512, 256)
        H = 16
        D = C // H
        key = jax.random.key(seed)
        k1, k2, k3, k4, k5 = jax.random.split(key, 5)
        s = 0.02
        return {'x': jax.random.normal(k1, (B, T, C), dtype=jnp.float32), 'W_qkv': jax.random.normal(k2, (C, 3 * C), dtype=jnp.float32) * s, 'b_qkv': jnp.zeros((3 * C,), dtype=jnp.float32), 'W_out': jax.random.normal(k3, (C, C), dtype=jnp.float32) * s, 'b_out': jnp.zeros((C,), dtype=jnp.float32)}
    _L0_attn_all = _L0_attn_setup()
    _L0_attn_in = {k: v for k, v in _L0_attn_all.items() if k in ('W_qkv', 'b_qkv', 'W_out', 'b_out')}
    del _L0_attn_all

    def _L0_ffn_setup():
        import jax, jax.numpy as jnp
        import numpy as np
        E, D, F, GATE_DIM = (8, 256, 1024, 16)
        B, T = (2, 512)
        key = jax.random.key(seed)
        ks = jax.random.split(key, 7)
        s = 0.02
        return {'hidden_states': jax.random.normal(ks[0], (B, T, D), dtype=jnp.float32), 'w_red': jax.random.normal(ks[1], (D, GATE_DIM), dtype=jnp.float32) * s, 'wg': jax.random.normal(ks[2], (E, GATE_DIM), dtype=jnp.float32), 'w1': jax.random.normal(ks[3], (E, D, F), dtype=jnp.float32) * s, 'b1': jax.random.normal(ks[4], (E, F), dtype=jnp.float32) * s, 'w2': jax.random.normal(ks[5], (E, F, D), dtype=jnp.float32) * s, 'b2': jax.random.normal(ks[6], (E, D), dtype=jnp.float32) * s}
    _L0_ffn_all = _L0_ffn_setup()
    _L0_ffn_in = {k: v for k, v in _L0_ffn_all.items() if k in ('w_red', 'wg', 'w1', 'b1', 'w2', 'b2')}
    del _L0_ffn_all
    return {'x': x, 'cls_tok': cls_tok, 'L0_tok_W_proj': _L0_tok_in['W_proj'], 'L0_tok_b_proj': _L0_tok_in['b_proj'], 'L0_tok_pos_emb': _L0_tok_in['pos_emb'], 'L0_attn_W_qkv': _L0_attn_in['W_qkv'], 'L0_attn_b_qkv': _L0_attn_in['b_qkv'], 'L0_attn_W_out': _L0_attn_in['W_out'], 'L0_attn_b_out': _L0_attn_in['b_out'], 'L0_ffn_w_red': _L0_ffn_in['w_red'], 'L0_ffn_wg': _L0_ffn_in['wg'], 'L0_ffn_w1': _L0_ffn_in['w1'], 'L0_ffn_b1': _L0_ffn_in['b1'], 'L0_ffn_w2': _L0_ffn_in['w2'], 'L0_ffn_b2': _L0_ffn_in['b2']}

def reference(x, cls_tok, L0_tok_W_proj, L0_tok_b_proj, L0_tok_pos_emb, L0_attn_W_qkv, L0_attn_b_qkv, L0_attn_W_out, L0_attn_b_out, L0_ffn_w_red, L0_ffn_wg, L0_ffn_w1, L0_ffn_b1, L0_ffn_w2, L0_ffn_b2):
    import jax
    import jax.numpy as jnp

    def _L0_tok_ref(images, W_proj, b_proj, pos_emb):
        import jax, jax.numpy as jnp
        import numpy as np
        P = 16
        E = 256

        def patchify(images, patch_size):
            B, H, W, C = images.shape
            hp, wp = (H // patch_size, W // patch_size)
            x = images.reshape(B, hp, patch_size, wp, patch_size, C)
            x = x.transpose(0, 1, 3, 2, 4, 5)
            return x.reshape(B, hp * wp, patch_size * patch_size * C)
        patches = patchify(images, P)
        out = jnp.einsum('bnd,ed->bne', patches, W_proj) + b_proj + pos_emb[None, :, :]
        return out

    def _L0_attn_ref(x, W_qkv, b_qkv, W_out, b_out):
        import jax, jax.numpy as jnp
        import numpy as np
        B, T, C = (2, 512, 256)
        H = 16
        D = C // H
        Bx, Tx, Cx = x.shape
        qkv = x @ W_qkv + b_qkv
        q, k, v = jnp.split(qkv, 3, axis=-1)

        def heads(t):
            return t.reshape(Bx, Tx, H, D).transpose(0, 2, 1, 3)
        q, k, v = (heads(q), heads(k), heads(v))
        att = jnp.einsum('bhtd,bhsd->bhts', q, k) / np.sqrt(D).astype(np.float32)
        causal = jnp.tril(jnp.ones((Tx, Tx), dtype=bool))
        att = jnp.where(causal[None, None], att, -jnp.inf)
        att = jax.nn.softmax(att, axis=-1)
        out = jnp.einsum('bhts,bhsd->bhtd', att, v)
        out = out.transpose(0, 2, 1, 3).reshape(Bx, Tx, Cx)
        return out @ W_out + b_out

    def _L0_ffn_ref(hidden_states, w_red, wg, w1, b1, w2, b2):
        import jax, jax.numpy as jnp
        import numpy as np
        E, D, F, GATE_DIM = (8, 256, 1024, 16)
        B, T = (2, 512)
        b, t, c = hidden_states.shape
        x = hidden_states.reshape(-1, c)
        red = x @ w_red
        wg_n = wg / jnp.maximum(jnp.linalg.norm(wg, axis=1, keepdims=True), 0.0001)
        logits = red @ wg_n.T
        gates = jax.nn.softmax(logits, axis=1)
        idx = jnp.argmax(gates, axis=1)
        scores = jnp.take_along_axis(gates, idx[:, None], axis=1)
        h = jax.nn.gelu(jnp.einsum('td,edf->etf', x, w1) + b1[:, None, :], approximate=False)
        y = jnp.einsum('etf,efd->etd', h, w2) + b2[:, None, :]
        out = jnp.take_along_axis(y, idx[None, :, None], axis=0)[0]
        out = out * scores
        return out.reshape(b, t, c)
    h = _L0_tok_ref(x, L0_tok_W_proj, L0_tok_b_proj, L0_tok_pos_emb)
    h = jnp.concatenate([jnp.broadcast_to(cls_tok, (h.shape[0], 1, h.shape[2])), h], axis=1)
    h = h + _L0_attn_ref(_layernorm(h, axis=-1), L0_attn_W_qkv, L0_attn_b_qkv, L0_attn_W_out, L0_attn_b_out)
    h = h + _L0_ffn_ref(_layernorm(h, axis=-1), L0_ffn_w_red, L0_ffn_wg, L0_ffn_w1, L0_ffn_b1, L0_ffn_w2, L0_ffn_b2)
    return h

_drawn_inputs = setup_inputs


def setup_inputs(seed=0):
    import zlib

    import numpy as np

    out = dict(_drawn_inputs(seed))
    spreads = {'L0_attn_b_qkv': (0.0, 0.1), 'L0_attn_b_out': (0.0, 0.1)}
    factors = {'cls_tok': 2.821,
     'L0_tok_b_proj': 2.733,
     'L0_tok_pos_emb': 2.832,
     'L0_ffn_w_red': 2.805,
     'L0_ffn_wg': 2.794,
     'L0_ffn_w1': 2.737,
     'L0_ffn_b1': 8.0,
     'L0_ffn_b2': 8.0}
    for name, (base, spread) in spreads.items():
        noise = np.random.default_rng([zlib.crc32(name.encode()), seed]).standard_normal(out[name].shape)
        drawn = base * np.exp(spread * noise) if base else spread * noise
        out[name] = jnp.asarray(drawn.astype(out[name].dtype))
    for name, factor in factors.items():
        out[name] = (out[name] * factor).astype(out[name].dtype)
    return out
```

```python
from contextlib import ExitStack

import numpy as np

import concourse.bass as bass
from concourse import mybir

ALU = mybir.AluOpType
ACT = mybir.ActivationFunctionType
F32 = mybir.dt.float32
BF16 = mybir.dt.bfloat16
U32 = mybir.dt.uint32
I32 = mybir.dt.int32
AX = mybir.AxisListType

B, PATCHES, D, HEADS, DH = 16, 36, 256, 16, 16
S = PATCHES + 1
T = B * S
P = 128
NT = -(-T // P)
TP = NT * P
TAIL = T - (NT - 1) * P
PD = 768
KE = PD // P
KD = D // P
HH = HEADS // KD
HS = HH * S
PAIRS = B // 2
UNITS = PAIRS * KD
ROW_B = 64
ROWS = ROW_B + S
GH = 3
CH = -(-HH // GH)
GS = GH * S
VW = DH + 1
VI = HEADS * VW
E, F = 8, 1024
FT = F // P
SLOTS = E * P
OVF = (T + E * (P - 1)) // P - E
RING = 4
EPS = 1e-5
FAR = 4096.0
NOROW = 1024

_F = {}
_at = 0
for _name, _n in (("ident", P), ("kmask", HH), ("vmask", 2 * HEADS), ("revidx", E), ("keyoff", NT),
                  ("valid", NT), ("thr", OVF), ("tri", E * E), ("tilenum", OVF), ("pow", 2),
                  ("iota", SLOTS)):
    _F[_name] = (_at, _at + _n)
    _at += _n
NF = _at
_B = {}
_at = 0
for _name, _n in (("ident", ROW_B), ("causal", HS), ("ones", P), ("before", P), ("token", 3 * NT)):
    _B[_name] = (_at, _at + _n)
    _at += _n
NB = _at

PROJ_AT = {2 * (-(-min(P * (j + 1), T) // (2 * S)) - 1) + 1 + 4: j for j in range(NT)}
STEPS = max(PROJ_AT) + 4


def constants():
    cf = np.zeros((P, NF), np.float32)
    p = np.arange(P)

    def put(name, v):
        a, b = _F[name]
        cf[:, a:b] = v

    put("ident", np.eye(P))
    put("kmask", p[:, None] // DH == np.arange(HH)[None])
    h = np.arange(2 * HEADS) % HH
    put("vmask", p[:, None] // S == (h % GH)[None])
    put("revidx", E - np.arange(E)[None])
    tok = p[:, None] + P * np.arange(NT)[None]
    put("keyoff", E * P + FAR * (tok >= T))
    put("valid", tok < T)
    put("thr", P * (1 + np.arange(OVF))[None])
    put("tri", (np.arange(E)[:, None] >= np.arange(E)[None]).reshape(1, -1))
    put("tilenum", np.arange(OVF)[None])
    put("pow", np.array([[-0.5, 0.5]]))
    put("iota", np.arange(SLOTS)[None])
    cb = np.zeros((P, NB), np.float32)

    def putb(name, v):
        a, b = _B[name]
        cb[:, a:b] = v

    putb("ident", np.eye(P)[:, :ROW_B])
    causal = np.where(np.arange(S)[None] <= p[:, None], 0.0, -1e30)
    putb("causal", np.tile(causal, (1, HH)))
    putb("ones", 1.0)
    putb("before", p[:, None] < p[None])
    putb("token", np.stack([tok // 8, tok % 8, np.ones_like(tok)], -1).reshape(P, -1))
    sel = np.zeros((S + 1, TP), np.float32)
    t = np.arange(T)
    sel[t % S, t] = 1.0
    sel[S, t] = t % S > 0
    return cf, cb.astype(np.dtype("bfloat16")), sel


def vit_tower(nc, embed_in, table, w_qkv, b_qk, b_v, w_out, b_out, wg, w_red_t, w1, b1, w2, b2,
              cf_d, cb_d, sel_d, out):
    ctx = ExitStack()
    with ctx:
        def sb(name, shape, dt=F32):
            return ctx.enter_context(nc.sbuf_tensor(name, shape, dt))

        def sem(name):
            return ctx.enter_context(nc.semaphore(name))

        hz_d = nc.dram_tensor("hz_scratch", [TP, 2 * D], F32, kind="Internal").ap()

        cf = sb("cf", [P, NF])
        cb = sb("cb", [P, NB], BF16)

        def C(name):
            a, b = _F[name]
            return cf[:, a:b]

        def CB(name):
            a, b = _B[name]
            return cb[:, a:b]

        ident = C("ident")
        sel = sb("sel", [S + 1, TP])
        tab = sb("tab", [S + 1, D])
        wqkv = sb("wqkv", [P, KD, 3 * D])
        wout = sb("wout", [P, KD, D])
        bqk = sb("bqk", [P, 2 * KD])
        bqs = sb("bqs", [P, KD])
        bv = sb("bv", [P, KD])
        bout = sb("bout", [P, D])
        b1s = sb("b1s", [P, E, FT])
        b1o = sb("b1o", [P, OVF, FT])
        b2s = sb("b2s", [P, E, D])
        b2o = sb("b2o", [P, OVF, D])
        wgs = sb("wgs", [E, 16])
        wgsq = sb("wgsq", [E, 16])
        wgn = sb("wgn", [E, 16])
        wgv = sb("wgv", [E, 4])
        wgnt = sb("wgnt", [16, E])
        wredt = sb("wredt", [16, D])
        G = sb("G", [P, KD, E])
        early = sb("early", [P, KE * (TP + D)])
        emb = early[:, :].rearrange("p (k n) -> p k n", k=KE)
        vbd = early[0:GS, 0:B * VI + VW]
        h = sb("h", [P, NT, D])
        xnt = sb("xnt", [P, KD, TP])
        qt = sb("qt", [P, KD, TP])
        kt = sb("kt", [P, KD, T])
        wide = sb("wide", [P, KD * B * HS])
        kbd = wide[:, :].rearrange("p (c b h s) -> p c b h s", c=KD, b=B, h=HH)
        place = wide[:, 0:NT * SLOTS // 2].bitcast(BF16).rearrange("p (j s) -> p j s", j=NT)
        shifted = sb("shifted", [ROWS, 2, HS])
        probs = sb("probs", [ROWS, 2, (HH + 1) * S])
        probst = sb("probst", [GS, 2, CH * ROWS])
        negmax = sb("negmax", [ROWS, 2, HH])
        rsum = sb("rsum", [ROWS, 2, HH])
        o = sb("o", [ROWS, 2, P])
        ot = sb("ot", [P, KD, TP])
        stats = sb("stats", [P, NT, 6])
        mv = sb("mv", [P, NT, 2])
        veps = sb("veps", [P, NT])
        rstd = sb("rstd", [P, NT])
        stats2 = sb("stats2", [P, NT, 6])
        mv2 = sb("mv2", [P, NT, 2])
        veps2 = sb("veps2", [P, NT])
        rstd2 = sb("rstd2", [P, NT])
        hz = sb("hz", [P, NT, 2 * D])
        xn = hz[:, :, D:2 * D]
        zt = sb("zt", [P, 2, KD, P])
        lg = sb("lg", [P, NT, E])
        lmax = sb("lmax", [P, NT])
        cand = sb("cand", [P, NT, E])
        prio = sb("prio", [P, NT, E])
        best = sb("best", [P, NT])
        hot = sb("hot", [P, NT, E])
        hotb = sb("hotb", [P, NT, E], BF16)
        low = sb("low", [P, NT, E])
        elow = sb("elow", [P, NT, E])
        esum = sb("esum", [P, NT])
        score = sb("score", [P, NT])
        rem = sb("rem", [P, 2, NT])
        info = sb("info", [P, NT, 6], BF16)
        rtmp = sb("rtmp", [P, NT, E])
        rank = sb("rank", [P, NT])
        kbase = sb("kbase", [P, NT])
        kover = sb("kover", [P, NT])
        ksum = sb("ksum", [P, NT])
        key = sb("key", [P, NT])
        NTILE = E + OVF
        inf = sb("inf", [P, NTILE, 6])
        rowf = sb("rowf", [P, NTILE])
        skip = sb("skip", [P, NTILE])
        growu = sb("growu", [P, NTILE], U32)
        srowu = sb("srowu", [P, NTILE], U32)
        sc2 = sb("sc2", [P, NTILE])
        slotscore = sb("slotscore", [P, NTILE])
        over = sb("over", [P, E, OVF])
        novf = sb("novf", [P, E])
        cnt = sb("cnt", [P, E])
        pre = sb("pre", [P, E, E])
        incl = sb("incl", [P, E])
        excl = sb("excl", [P, E])
        tcmp = sb("tcmp", [P, OVF, E])
        teid = sb("teid", [P, OVF + 1])
        meta = sb("meta", [P, OVF + 1], I32)
        tbase = sb("tbase", [P, NT])
        okey = sb("okey", [P, 3, NT])
        at = [0]

        def late(n):
            at[0] += n
            return early[:, at[0] - n:at[0]]

        rows = late(RING * 2 * D).rearrange("p (r n) -> p r n", r=RING)
        gt = late(2 * FT * P).rearrange("p (b f n) -> p b f n", b=2, f=FT)
        xt = late(2 * KD * P).rearrange("p (b k n) -> p b k n", b=2, k=KD)
        yout = late(2 * D).rearrange("p (b n) -> p b n", b=2)
        ysum = sb("ysum", [P, 2, D])
        w1s = sb("w1s", [P, RING, KD, F])
        w2s = sb("w2s", [P, RING, FT, D])
        thrice = [w[:, RING - 1, :, :].rearrange("p a b -> p (a b)")[:, 0:B * GS] for w in (w1s, w2s)]

        ps = ctx.enter_context(nc.psum_tensor("ps", [P, 8, 512], F32))
        BS, BP, BO, BV, BZ = 0, 2, 4, 6, 7
        cum = ps[:, 5, 64:64 + NT * E].rearrange("p (j e) -> p j e", e=E)
        cntp = ps[:, 5, 112:112 + E]
        lgp = [ps[:, bank, 320:320 + NT * E].rearrange("p (j e) -> p j e", e=E) for bank in (BZ, BV)]
        EARLY = 2
        infp = ps[:, 4, 128:128 + 6 * (E + OVF)].rearrange("p (t c) -> p t c", c=6)

        names = """loaded_sel loaded_tab loaded_cf loaded_cb loaded_wqkv loaded_wout loaded_bqk
            loaded_bv loaded_bout loaded_b1 loaded_b2 loaded_wg loaded_wred
            embedded h_saved veps_ready rstd_ready xn_ready xnt_ps xnt_ready thrice_ready
            wg_sq wg_norm wgn_ready wgnt_ps wgnt_ready g_ps g_ready bqs_ready
            qk_ps k_ready q_ready kbd_dve kbd_act v_zeroed v_ps v_ready pads_ready
            scores_ps shifted_ready probs_ready probst_ps probst_ready o_ps o_ready ot_ps ot_ready
            hb_ready proj_ps veps2_ready rstd2_ready h2_ready z_ready zt_ps zt_ready logits_ps
            hz_stored hot_ready low_ready elow_ready cum_ps info_ready place_ready info_ps slots_ready
            xt_ps xt_ready hidden_ps gelu_ready y_ps y_ready
            meta_ready oplace_ready oinfo_ps oslots_ready
            dve_chain""".split()
        q = {n: sem(n) for n in names}
        loaded_emb = [sem(f"loaded_emb{k}") for k in range(KE)]
        loaded_w = [sem(f"loaded_w{r}") for r in range(RING)]
        scattered = [sem(f"scattered{b}") for b in range(2)]
        gathered = [sem(f"gathered{r}") for r in range(RING)]

        block = ctx.enter_context(nc.Block())

        def used_columns(ap):
            return ap.rearrange("p (a s) -> p a s", a=2)[:, :, 0:S]

        def tile_of(t):
            b1t = b1s[:, t, :] if t < E else b1o[:, t - E, :]
            b2t = b2s[:, t, :] if t < E else b2o[:, t - E, :]
            return t % RING, b1t, b2t

        @block.sync
        def _(sp):
            for k in range(KE):
                sp.dma_start(emb[:, k, :], embed_in[k]).then_inc(loaded_emb[k], 16)
            sp.dma_start(wqkv[:, :, :], w_qkv.rearrange("(k p) n -> p k n", p=P)).then_inc(q["loaded_wqkv"], 16)
            sp.dma_start(wout[:, :, :], w_out.rearrange("(k p) n -> p k n", p=P)).then_inc(q["loaded_wout"], 16)

            def load_expert(t):
                r = t % RING
                if t >= RING:
                    sp.wait_ge(q["y_ps"], t - RING + 1)
                sp.dma_start(w1s[:, r, :, :], w1[t].rearrange("(k p) f -> p k f", p=P)).then_inc(loaded_w[r], 16)
                sp.dma_start(w2s[:, r, :, :], w2[t].rearrange("(k p) d -> p k d", p=P)).then_inc(loaded_w[r], 16)

            for t in range(RING - 1):
                load_expert(t)
            for j in range(NT):
                if j == 2:
                    sp.wait_ge(q["v_ps"], PAIRS)
                    load_expert(RING - 1)
                sp.wait_ge(q["z_ready"], j + 1)
                sp.dma_start(hz_d[j * P:(j + 1) * P, :], hz[:, j, :]).then_inc(q["hz_stored"], 16)
            for t in range(RING, E):
                load_expert(t)
            sp.wait_ge(q["meta_ready"], 1)
            n = sp.value_load(meta[0:1, OVF:OVF + 1], min_val=0, max_val=OVF)
            for i in range(OVF):
                with sp.If(n > i):
                    e = sp.value_load(meta[0:1, i:i + 1], min_val=0, max_val=E - 1)
                    r = (E + i) % RING
                    sp.wait_ge(q["y_ps"], E + i - RING + 1)
                    sp.dma_start(w1s[:, r, :, :],
                                 w1[bass.ds(e, 1)].rearrange("o (k p) f -> p (o k) f", p=P)).then_inc(loaded_w[r], 16)
                    sp.dma_start(w2s[:, r, :, :],
                                 w2[bass.ds(e, 1)].rearrange("o (k p) d -> p (o k) d", p=P)).then_inc(loaded_w[r], 16)
                    sp.dma_start(b1o[:, i, :],
                                 b1[bass.ds(e, 1)].rearrange("o p f -> p (o f)")).then_inc(loaded_w[r], 16)
                    sp.dma_start(b2o[:, i, :], b2[bass.ds(e, 1)].partition_broadcast(P).rearrange("p o d -> p (o d)"))\
                      .then_inc(loaded_w[r], 16)
            for b in range(2):
                sp.wait_ge(scattered[b], 16 * E // 2)

        @block.scalar
        def _(act):
            act.dma_start(sel[:, :], sel_d).then_inc(q["loaded_sel"], 16)
            act.dma_start(tab[:, :], table).then_inc(q["loaded_tab"], 16)
            act.dma_start(cf[:, :], cf_d).then_inc(q["loaded_cf"], 16)
            act.dma_start(wgs[:, :], wg).then_inc(q["loaded_wg"], 16)
            act.dma_start(wredt[:, :], w_red_t).then_inc(q["loaded_wred"], 16)
            act.dma_start(cb[:, :], cb_d).then_inc(q["loaded_cb"], 16)
            act.dma_start(bqk[:, :], b_qk).then_inc(q["loaded_bqk"], 16)
            act.dma_start(bv[:, :], b_v).then_inc(q["loaded_bv"], 16)
            act.dma_start(bout[:, :], b_out.partition_broadcast(P)).then_inc(q["loaded_bout"], 16)
            act.dma_start(b1s[:, :, :], b1.rearrange("e p f -> p e f")).then_inc(q["loaded_b1"], 16)
            act.dma_start(b2s[:, :, :], b2.partition_broadcast(P)).then_inc(q["loaded_b2"], 16)
            for j in range(NT):
                act.wait_ge(q["embedded"], j + 1)
                nc.scalar.activation(h[:, j, :], ps[:, j, 0:D], ACT.Copy).then_inc(q["h_saved"], 1)
            for j in range(NT):
                act.wait_ge(q["xnt_ps"], j + 1)
                nc.scalar.activation(xnt[:, :, j * P:(j + 1) * P],
                                     ps[:, 5 + 2 * (j % 2), 0:KD * P].rearrange("p (k n) -> p k n", k=KD),
                                     ACT.Copy).then_inc(q["xnt_ready"], 1)
            act.wait_ge(q["xnt_ready"], NT)
            for k in range(KD):
                nc.scalar.activation(thrice[k].rearrange("p (b r s) -> p b r s", r=GH, s=S),
                                     xnt[:, k, 0:T].rearrange("p (b s) -> p b s", s=S).unsqueeze(2)
                                     .to_broadcast([P, B, GH, S]), ACT.Copy).then_inc(q["thrice_ready"], 1)
            act.wait_ge(q["bqs_ready"], 1)
            act.wait_ge(q["pads_ready"], 1)
            for c in range(KD):
                act.wait_ge(q["qk_ps"], KD + c + 1)
                nc.scalar.activation(qt[:, c, 0:T].rearrange("p (a n) -> p a n", a=2),
                                     ps[:, 2 + 2 * c:4 + 2 * c, 0:T // 2],
                                     ACT.Identity, bias=bqs[:, c:c + 1], scale=DH ** -0.5).then_inc(q["q_ready"], 1)
            act.wait_ge(q["k_ready"], 2)
            act.wait_ge(q["loaded_cf"], 16)
            for hd in range(5, HH):
                nc.scalar.activation(kbd[:, 1, :, hd, :], kt[:, 1, :].rearrange("p (b s) -> p b s", s=S), ACT.Copy,
                                     scale=C("kmask")[:, hd:hd + 1]).then_inc(q["kbd_act"], 1)
            act.wait_ge(q["loaded_bv"], 16)
            zj = 0
            for i in range(STEPS):
                if i < UNITS:
                    act.wait_ge(q["shifted_ready"], i + 1)
                    if i >= 2:
                        act.wait_ge(q["probst_ps"], i - 1)
                    nc.scalar.activation(probs[:, i % 2, 0:HS], shifted[:, i % 2, :], ACT.Exp).then_inc(q["probs_ready"], 1)
                if 0 <= i - 1 < UNITS:
                    u = i - 1
                    act.wait_ge(q["probst_ps"], u + 1)
                    if u >= 2:
                        act.wait_ge(q["o_ps"], u - 1)
                    nc.scalar.activation(probst[:, u % 2, :], ps[0:GS, BP + u % 2, 0:CH * ROWS], ACT.Copy)\
                        .then_inc(q["probst_ready"], 1)
                if 0 <= i - 3 < UNITS:
                    u = i - 3
                    pair, c = u // 2, u % 2
                    act.wait_ge(q["ot_ps"], u + 1)
                    src = used_columns(ps[:, BO + u % 2, 320:320 + 2 * ROW_B])
                    nc.scalar.activation(ot[:, c, pair * 2 * S:(pair + 1) * 2 * S].rearrange("p (a s) -> p a s", a=2),
                                         src, ACT.Identity, bias=bv[:, c:c + 1]).then_inc(q["ot_ready"], 1)
                if i - 2 in PROJ_AT:
                    j = PROJ_AT[i - 2]
                    act.wait_ge(q["zt_ps"], j + 1)
                    if j >= 2:
                        act.wait_ge(q["logits_ps"], j - 1)
                    nc.scalar.activation(zt[:, j % 2, :, :],
                                         ps[:, BZ, 0:KD * P].rearrange("p (k n) -> p k n", k=KD),
                                         ACT.Copy).then_inc(q["zt_ready"], 1)
            act.wait_ge(q["low_ready"], 1)
            nc.scalar.activation(elow[:, :, :], low[:, :, :], ACT.Exp).then_inc(q["elow_ready"], 1)
            act.wait_ge(q["loaded_b1"], 16)

            def gelu(t):
                b1t = tile_of(t)[1]
                if t >= 2:
                    act.wait_ge(q["y_ps"], t - 1)
                for f in range(FT):
                    if f % 4 == 0:
                        act.wait_ge(q["hidden_ps"], 2 * t + f // 4 + 1)
                    nc.scalar.activation(gt[:, t % 2, f, :],
                                         ps[:, 2 * (t % 2) + f // 4, (f % 4) * P:(f % 4 + 1) * P],
                                         ACT.Gelu, bias=b1t[:, f:f + 1]).then_inc(q["gelu_ready"], 1)

            for t in range(E):
                gelu(t)
            act.wait_ge(q["meta_ready"], 1)
            n = act.value_load(meta[0:1, OVF:OVF + 1], min_val=0, max_val=OVF)
            for i in range(OVF):
                with act.If(n > i):
                    act.wait_ge(loaded_w[i % RING], 32 * 2 + 64)
                    gelu(E + i)

        @block.tensor
        def _(pe):
            pe.wait_ge(q["wgn_ready"], 1)
            nc.tensor.transpose(ps[0:16, BZ, 0:E], wgn[:, :], ident[0:E, 0:E]).then_inc(q["wgnt_ps"], 1)
            pe.wait_ge(q["wgnt_ready"], 1)
            pe.wait_ge(q["loaded_wred"], 16)
            for k in range(KD):
                m = nc.tensor.matmul(ps[:, BZ, 16 + k * E:16 + (k + 1) * E], wredt[:, k * P:(k + 1) * P], wgnt[:, :],
                                     start=True, stop=True)
            m.then_inc(q["g_ps"], 1)
            pe.wait_ge(q["g_ready"], 1)
            pe.wait_ge(q["loaded_sel"], 16)
            pe.wait_ge(q["loaded_tab"], 16)
            for j in range(NT):
                nc.tensor.matmul(ps[:, j, 0:D], sel[:, j * P:(j + 1) * P], tab[:, :], start=True, stop=False)
            def embed(k, j):
                return nc.tensor.matmul(ps[:, j, 0:D], emb[:, k, j * P:(j + 1) * P], emb[:, k, TP:TP + D],
                                        start=False, stop=(k == KE - 1))

            for k in range(KE - 3):
                pe.wait_ge(loaded_emb[k], 16)
                for j in range(NT):
                    embed(k, j)
            for k in range(KE - 3, KE):
                pe.wait_ge(loaded_emb[k], 16)
            for j in range(NT):
                for k in range(KE - 3, KE):
                    m = embed(k, j)
                m.then_inc(q["embedded"], 1)
            def turn_normalised(j):
                pe.wait_ge(q["xn_ready"], j + 1)
                if j >= 2:
                    pe.wait_ge(q["xnt_ready"], j - 1)
                for k in range(KD):
                    m = nc.tensor.transpose(ps[:, 5 + 2 * (j % 2), k * P:(k + 1) * P], xn[:, j, k * P:(k + 1) * P], ident)
                m.then_inc(q["xnt_ps"], 1)
            HALF = T // 2
            for j in range(-(-HALF // P)):
                turn_normalised(j)
            pe.wait_ge(q["loaded_wqkv"], 16)
            pe.wait_ge(q["h_saved"], NT)
            pe.wait_ge(q["g_ready"], 1)
            pe.wait_ge(q["xnt_ready"], -(-HALF // P))
            for a in range(2):
                for n, (col, bank) in enumerate(((D, 0), (D + P, 6), (0, 2), (P, 4))):
                    for k in range(KD):
                        m = nc.tensor.matmul(ps[:, bank + a, 0:HALF], wqkv[:, k, col:col + P],
                                             xnt[:, k, a * HALF:(a + 1) * HALF], start=(k == 0), stop=(k == KD - 1))
                    if a:
                        m.then_inc(q["qk_ps"], 1)
                if a == 0:
                    for j in range(-(-HALF // P), NT):
                        turn_normalised(j)
                    pe.wait_ge(q["xnt_ready"], NT)

            def values(pair):
                if pair >= 1:
                    pe.wait_ge(q["v_ready"], pair)
                else:
                    pe.wait_ge(q["k_ready"], 2)
                    pe.wait_ge(q["thrice_ready"], KD)
                for a in range(2):
                    t0 = (2 * pair + a) * GS
                    for k in range(KD):
                        lhs = thrice[k][:, t0:t0 + GS]
                        m = nc.tensor.matmul(ps[0:GS, BV, a * D:(a + 1) * D], lhs, wqkv[:, k, 2 * D:3 * D],
                                             start=(k == 0), stop=(k == KD - 1))
                m.then_inc(q["v_ps"], 1)

            def scores(u):
                pair, c = u // 2, u % 2
                bank = BS + u % 2
                if u < 2:
                    pe.wait_ge(q["q_ready"], u + 1)
                    pe.wait_ge(q["kbd_dve"], (HH, HH + 5)[u])
                    if u:
                        pe.wait_ge(q["kbd_act"], HH - 5)
                else:
                    pe.wait_ge(q["shifted_ready"], u - 1)
                for a, w in ((0, ROW_B), (1, S)):
                    t0 = (2 * pair + a) * S
                    nc.tensor.matmul(ps[a * ROW_B:a * ROW_B + w, bank, 0:HS], qt[:, c, t0:t0 + w],
                                     kbd[:, c, 2 * pair + a, :, :].rearrange("p h s -> p (h s)"), start=True, stop=False)
                for a, w in ((0, ROW_B), (1, S)):
                    m = nc.tensor.matmul(ps[a * ROW_B:a * ROW_B + w, bank, 0:HS], CB("ident")[0:S, 0:w],
                                         CB("causal")[0:S, :], start=False, stop=True)
                m.then_inc(q["scores_ps"], 1)

            def transposed(u):
                pe.wait_ge(q["probs_ready"], u + 1)
                if u >= 2:
                    pe.wait_ge(q["probst_ready"], u - 1)
                for g in range(CH):
                    m = nc.tensor.transpose(ps[0:GS, BP + u % 2, g * ROWS:(g + 1) * ROWS],
                                            probs[:, u % 2, g * GS:(g + 1) * GS], ident[0:ROWS, 0:ROWS])
                m.then_inc(q["probst_ps"], 1)

            def attend(u):
                pair, c = u // 2, u % 2
                pe.wait_ge(q["probst_ready"], u + 1)
                pe.wait_ge(q["v_ready"], pair + 1)
                if u >= 2:
                    pe.wait_ge(q["ot_ready"], u - 1)
                for g in range(CH):
                    col = 2 * pair * VI + (c * HH + g * GH) * VW
                    rhs = early[0:GS, col:col + 2 * VI].rearrange("p (a n) -> p a n", a=2)[:, :, 0:GH * VW]
                    dst = ps[0:ROWS, BO + u % 2, 0:2 * CH * GH * VW].rearrange("p (a n) -> p a n", a=2)
                    m = nc.tensor.matmul(dst[:, :, g * GH * VW:(g + 1) * GH * VW],
                                         probst[:, u % 2, g * ROWS:(g + 1) * ROWS], rhs, start=True, stop=True)
                m.then_inc(q["o_ps"], 1)

            def turned(u):
                pe.wait_ge(q["o_ready"], u + 1)
                nc.tensor.transpose(ps[:, BO + u % 2, 320:320 + ROWS], o[:, u % 2, :], ident[0:ROWS, 0:ROWS])\
                    .then_inc(q["ot_ps"], 1)

            pe.wait_ge(q["loaded_cb"], 16)
            pe.wait_ge(q["pads_ready"], 1)
            values(0)
            for i in range(STEPS):
                if i < UNITS:
                    scores(i)
                    if i % 2 == 0 and i // 2 + 1 < PAIRS:
                        values(i // 2 + 1)
                if 0 <= i - 1 < UNITS:
                    transposed(i - 1)
                if 0 <= i - 2 < UNITS:
                    attend(i - 2)
                if 0 <= i - 3 < UNITS:
                    turned(i - 3)
                if i - 3 in PROJ_AT:
                    j = PROJ_AT[i - 3]
                    pe.wait_ge(q["zt_ready"], j + 1)
                    if j == EARLY:
                        pe.wait_ge(q["v_ready"], PAIRS)
                    for k in range(KD):
                        m = nc.tensor.matmul(lgp[j >= EARLY][:, j, :], zt[:, j % 2, k, :], G[:, k, :],
                                             start=(k == 0), stop=(k == KD - 1))
                    m.then_inc(q["logits_ps"], 1)
                if i - 2 in PROJ_AT:
                    j = PROJ_AT[i - 2]
                    pe.wait_ge(q["z_ready"], j + 1)
                    for k in range(KD):
                        m = nc.tensor.transpose(ps[:, BZ, k * P:(k + 1) * P],
                                                hz[:, j, D + k * P:D + (k + 1) * P], ident)
                    m.then_inc(q["zt_ps"], 1)
                if i in PROJ_AT:
                    j = PROJ_AT[i]
                    if j == 0:
                        pe.wait_ge(q["loaded_wout"], 16)
                    else:
                        pe.wait_ge(q["zt_ready"], j)
                    pe.wait_ge(q["ot_ready"], i - 3)
                    for k in range(KD):
                        m = nc.tensor.matmul(ps[:, BZ, 0:D], ot[:, k, j * P:(j + 1) * P], wout[:, k, :],
                                             start=(k == 0), stop=(k == KD - 1))
                    m.then_inc(q["proj_ps"], 1)
            pe.wait_ge(q["hot_ready"], 1)
            hot_flat = hotb[:, :, :].rearrange("p j e -> p (j e)")
            nc.tensor.matmul(cum.rearrange("p j e -> p (j e)"), CB("before"), hot_flat, start=True, stop=False)
            for i in range(NT - 1):
                m = nc.tensor.matmul(cum[:, i + 1:NT, :], CB("ones"),
                                     hotb[:, i, :].unsqueeze(1).to_broadcast([P, NT - 1 - i, E]),
                                     start=False, stop=(i == NT - 2))
            for j in range(NT):
                m = nc.tensor.matmul(cntp, CB("ones"), hotb[:, j, :], start=(j == 0), stop=(j == NT - 1))
            m.then_inc(q["cum_ps"], 1)

            def slot_info(t, c):
                for j in range(NT):
                    m = nc.tensor.matmul(infp[:, t, :], place[:, j, c:c + P], info[:, j, :],
                                         start=(j == 0), stop=(j == NT - 1))
                return m

            pe.wait_ge(q["info_ready"], 1)
            for part, (t0, t1) in enumerate(((0, 2), (2, E))):
                pe.wait_ge(q["place_ready"], part + 1)
                for t in range(t0, t1):
                    m = slot_info(t, t * P)
                m.then_inc(q["info_ps"], 1)

            def turn_rows(t):
                pe.wait_ge(gathered[t % RING], 16 * (t // RING + 1))
                if t >= 2:
                    pe.wait_ge(q["xt_ready"], t - 1)
                for k in range(KD):
                    m = nc.tensor.transpose(ps[:, 6 + t % 2, k * P:(k + 1) * P],
                                            rows[:, t % RING, D + k * P:D + (k + 1) * P], ident)
                m.then_inc(q["xt_ps"], 1)

            def hidden(t):
                r = t % RING
                pe.wait_ge(loaded_w[r], 32 * (t // RING + 1) + (32 if t >= E else 0))
                pe.wait_ge(q["xt_ready"], t + 1)
                if t >= 2:
                    pe.wait_ge(q["gelu_ready"], FT * (t - 1))
                for f in range(FT):
                    for k in range(KD):
                        m = nc.tensor.matmul(ps[:, 2 * (t % 2) + f // 4, (f % 4) * P:(f % 4 + 1) * P],
                                             w1s[:, r, k, f * P:(f + 1) * P], xt[:, t % 2, k, :],
                                             start=(k == 0), stop=(k == KD - 1))
                    if f % 4 == 3:
                        m.then_inc(q["hidden_ps"], 1)

            def down(t):
                r = t % RING
                if t >= 2:
                    pe.wait_ge(q["y_ready"], t - 1)
                for f in range(FT):
                    pe.wait_ge(q["gelu_ready"], FT * t + f + 1)
                    m = nc.tensor.matmul(ps[:, 4 + t % 2, 0:D], gt[:, t % 2, f, :], w2s[:, r, f, :],
                                         start=(f == 0), stop=(f == FT - 1))
                m.then_inc(q["y_ps"], 1)

            turn_rows(0)
            hidden(0)
            turn_rows(1)
            for t in range(1, E):
                hidden(t)
                if t + 1 < E:
                    turn_rows(t + 1)
                down(t - 1)
            down(E - 1)
            pe.wait_ge(q["meta_ready"], 1)
            n = pe.value_load(meta[0:1, OVF:OVF + 1], min_val=0, max_val=OVF)
            with pe.If(n > 0):
                pe.wait_ge(q["oplace_ready"], 1)
                pe.wait_ge(q["y_ready"], E - 1)
                for i in range(OVF):
                    m = slot_info(E + i, i * P)
                m.then_inc(q["oinfo_ps"], 1)
            for i in range(OVF):
                with pe.If(n > i):
                    turn_rows(E + i)
                    hidden(E + i)
                    down(E + i)

        @block.vector
        def _(dve):
            chain = [0]

            def link(ins):
                chain[0] += 1
                ins.then_inc(q["dve_chain"], 1)
                dve.wait_ge(q["dve_chain"], chain[0])

            V = nc.vector
            dve.wait_ge(q["loaded_wg"], 16)
            link(V.tensor_tensor(wgsq[:, :], wgs[:, :], wgs[:, :], ALU.mult))
            V.tensor_reduce(wgv[:, 0:1], wgsq[:, :], AX.X, ALU.add).then_inc(q["wg_sq"], 1)
            dve.wait_ge(q["wg_norm"], 1)
            link(V.tensor_scalar(wgv[:, 2:3], wgv[:, 1:2], 1e-4, None, ALU.max))
            link(V.reciprocal(wgv[:, 3:4], wgv[:, 2:3]))
            V.tensor_scalar(wgn[:, :], wgs[:, :], wgv[:, 3:4], None, ALU.mult).then_inc(q["wgn_ready"], 1)
            dve.wait_ge(q["loaded_bqk"], 16)
            V.tensor_scalar(bqs[:, :], bqk[:, 0:KD], DH ** -0.5, None, ALU.mult).then_inc(q["bqs_ready"], 1)

            def norm_stats(src, st, m, ve, j, signal):
                link(V.bn_stats(st[:, j, :], src))
                link(V.bn_aggr(m[:, j, :], st[:, j, :]))
                V.tensor_scalar(ve[:, j:j + 1], m[:, j, 1:2], EPS, None, ALU.add).then_inc(signal, 1)

            def norm_apply(dst, src, m, rs, j):
                return V.tensor_scalar(dst, src, m[:, j, 0:1], rs[:, j:j + 1], ALU.subtract, ALU.mult)

            dve.wait_ge(q["wgnt_ps"], 1)
            V.tensor_copy(wgnt[:, :], ps[0:16, BZ, 0:E]).then_inc(q["wgnt_ready"], 1)
            dve.wait_ge(q["g_ps"], 1)
            V.tensor_copy(G[:, :, :], ps[:, BZ, 16:16 + KD * E].rearrange("p (k e) -> p k e", e=E))\
                .then_inc(q["g_ready"], 1)
            for j in range(NT + 1):
                if j < NT:
                    dve.wait_ge(q["h_saved"], j + 1)
                    norm_stats(h[:, j, :], stats, mv, veps, j, q["veps_ready"])
                if j:
                    dve.wait_ge(q["rstd_ready"], j)
                    norm_apply(xn[:, j - 1, :], h[:, j - 1, :], mv, rstd, j - 1).then_inc(q["xn_ready"], 1)
            for c in range(KD):
                dve.wait_ge(q["qk_ps"], c + 1)
                V.tensor_scalar(kt[:, c, :].rearrange("p (a n) -> p a n", a=2), ps[:, 6 * c:6 * c + 2, 0:T // 2],
                                bqk[:, KD + c:KD + c + 1], None, ALU.add).then_inc(q["k_ready"], 1)
                dve.wait_ge(q["k_ready"], c + 1)
                for hd in range(HH if c == 0 else 5):
                    V.tensor_scalar(kbd[:, c, :, hd, :], kt[:, c, :].rearrange("p (b s) -> p b s", s=S),
                                    C("kmask")[:, hd:hd + 1], None, ALU.mult).then_inc(q["kbd_dve"], 1)

            def values(pair):
                if pair == 0:
                    dve.wait_ge(q["v_zeroed"], 2)
                dve.wait_ge(q["v_ps"], pair + 1)
                V.tensor_tensor(
                    vbd[:, 2 * pair * VI:2 * (pair + 1) * VI].rearrange("p (h w) -> p h w", w=VW)[:, :, 0:DH],
                    ps[0:GS, BV, :].rearrange("p (h w) -> p h w", w=DH),
                    C("vmask")[0:GS, :].unsqueeze(2).to_broadcast([GS, 2 * HEADS, DH]), ALU.mult).then_inc(q["v_ready"], 1)

            values(0)
            for i in range(STEPS):
                if i < UNITS:
                    s3 = ps[0:ROWS, BS + i % 2, 0:HS].rearrange("p (h s) -> p h s", s=S)
                    dve.wait_ge(q["scores_ps"], i + 1)
                    link(V.tensor_reduce(negmax[:, i % 2, :], s3, AX.X, ALU.max, negate=True))
                    if i >= 2:
                        dve.wait_ge(q["probs_ready"], i - 1)
                    V.tensor_tensor(shifted[:, i % 2, :].rearrange("p (h s) -> p h s", s=S), s3,
                                    negmax[:, i % 2, :].unsqueeze(2).to_broadcast([ROWS, HH, S]), ALU.add)\
                        .then_inc(q["shifted_ready"], 1)
                    if i % 2 == 0 and i // 2 + 1 < PAIRS:
                        values(i // 2 + 1)
                if 0 <= i - 2 < UNITS:
                    u = i - 2
                    o4 = ps[0:ROWS, BO + u % 2, 0:2 * CH * GH * VW].rearrange("p (a h w) -> p a h w", a=2, w=VW)
                    dve.wait_ge(q["o_ps"], u + 1)
                    link(V.reciprocal(rsum[:, u % 2, :], o4[:, 0, 0:HH, DH:VW].rearrange("p h w -> p (h w)")))
                    if u >= 2:
                        dve.wait_ge(q["ot_ps"], u - 1)
                    for a, (r0, r1) in enumerate(((0, ROW_B), (ROW_B, ROWS))):
                        m = V.tensor_tensor(o[r0:r1, u % 2, :].rearrange("p (h w) -> p h w", w=DH),
                                            o4[r0:r1, a, 0:HH, 0:DH],
                                            rsum[r0:r1, u % 2, :].unsqueeze(2).to_broadcast([r1 - r0, HH, DH]), ALU.mult)
                        if a == 0:
                            link(m)
                    m.then_inc(q["o_ready"], 1)
                if i in PROJ_AT:
                    j = PROJ_AT[i]
                    dve.wait_ge(q["proj_ps"], j + 1)
                    dve.wait_ge(q["hb_ready"], j + 1)
                    V.tensor_tensor(hz[:, j, 0:D], ps[:, BZ, 0:D], h[:, j, :], ALU.add).then_inc(q["h2_ready"], 1)
                    dve.wait_ge(q["h2_ready"], j + 1)
                    norm_stats(hz[:, j, 0:D], stats2, mv2, veps2, j, q["veps2_ready"])
                if i - 1 in PROJ_AT:
                    j = PROJ_AT[i - 1]
                    dve.wait_ge(q["rstd2_ready"], j + 1)
                    norm_apply(hz[:, j, D:2 * D], hz[:, j, 0:D], mv2, rstd2, j).then_inc(q["z_ready"], 1)

            over_e = lambda ap: ap.unsqueeze(2).to_broadcast([P, NT, E])
            over_j = lambda ap: ap.unsqueeze(1).to_broadcast([P, NT, E])
            dve.wait_ge(q["logits_ps"], NT)
            V.tensor_copy(lg[:, 0:EARLY, :], lgp[0][:, 0:EARLY, :])
            link(V.tensor_copy(lg[:, EARLY:NT, :], lgp[1][:, EARLY:NT, :]))
            link(V.tensor_reduce(lmax[:, :], lg[:, :, :], AX.X, ALU.max))
            link(V.tensor_tensor(cand[:, :, :], lg[:, :, :], over_e(lmax[:, :]), ALU.is_equal))
            link(V.tensor_tensor(prio[:, :, :], cand[:, :, :], over_j(C("revidx")), ALU.mult))
            link(V.tensor_reduce(best[:, :], prio[:, :, :], AX.X, ALU.max))
            link(V.tensor_tensor(cand[:, :, :], over_j(C("revidx")), over_e(best[:, :]), ALU.is_equal))
            V.tensor_tensor(hotb[:, :, :], cand[:, :, :], over_e(C("valid")), ALU.mult).then_inc(q["hot_ready"], 1)
            V.tensor_tensor(hot[:, :, :], cand[:, :, :], over_e(C("valid")), ALU.mult)
            link(V.tensor_tensor(low[:, :, :], lg[:, :, :], over_e(lmax[:, :]), ALU.subtract))
            V.scalar_tensor_tensor(kbase[:, :], best[:, :], -float(P), C("keyoff"), ALU.mult, ALU.add)\
                .then_inc(q["low_ready"], 1)
            dve.wait_ge(q["cum_ps"], 1)
            V.tensor_copy(cnt[:, :], cntp)
            link(V.tensor_tensor(rtmp[:, :, :], cum, hot[:, :, :], ALU.mult))
            link(V.tensor_reduce(rank[:, :], rtmp[:, :, :], AX.X, ALU.add))
            V.tensor_scalar(kover[:, :], rank[:, :], float(P), FAR, ALU.is_ge, ALU.mult)
            link(V.tensor_tensor(ksum[:, :], rank[:, :], kbase[:, :], ALU.add))
            link(V.tensor_tensor(key[:, :], ksum[:, :], kover[:, :], ALU.add))

            def places(c0, c1):
                for j in range(NT):
                    m = V.tensor_scalar(place[:, j, c0:c1], C("iota")[:, c0:c1], key[:, j:j + 1], None, ALU.is_equal)
                m.then_inc(q["place_ready"], 1)

            places(0, 2 * P)
            dve.wait_ge(q["elow_ready"], 1)
            link(V.tensor_reduce(esum[:, :], elow[:, :, :], AX.X, ALU.add))
            link(V.reciprocal(score[:, :], esum[:, :]))
            V.tensor_copy(info[:, :, 0:3], CB("token").rearrange("p (j c) -> p j c", c=3))
            link(V.tensor_copy(info[:, :, 3], score[:, :]))
            link(V.tensor_tensor(rem[:, 0, :], score[:, :], info[:, :, 3], ALU.subtract))
            link(V.tensor_copy(info[:, :, 4], rem[:, 0, :]))
            link(V.tensor_tensor(rem[:, 1, :], rem[:, 0, :], info[:, :, 4], ALU.subtract))
            V.tensor_copy(info[:, :, 5], rem[:, 1, :]).then_inc(q["info_ready"], 1)

            def slots(t0, t1, signal):
                link(V.tensor_copy(inf[:, t0:t1, :], infp[:, t0:t1, :]))
                V.scalar_tensor_tensor(rowf[:, t0:t1], inf[:, t0:t1, 0], 8.0, inf[:, t0:t1, 1], ALU.mult, ALU.add)
                V.tensor_scalar(skip[:, t0:t1], inf[:, t0:t1, 2], -float(NOROW), float(NOROW), ALU.mult, ALU.add)
                link(V.tensor_tensor(sc2[:, t0:t1], inf[:, t0:t1, 3], inf[:, t0:t1, 4], ALU.add))
                V.tensor_tensor(slotscore[:, t0:t1], sc2[:, t0:t1], inf[:, t0:t1, 5], ALU.add)
                link(V.tensor_tensor(srowu[:, t0:t1], rowf[:, t0:t1], skip[:, t0:t1], ALU.add))
                V.tensor_copy(growu[:, t0:t1], rowf[:, t0:t1]).then_inc(signal, 1)

            dve.wait_ge(q["info_ps"], 1)
            slots(0, 2, q["slots_ready"])
            places(2 * P, SLOTS)
            dve.wait_ge(q["info_ps"], 2)
            slots(2, E, q["slots_ready"])

            def overflow():
                link(V.tensor_tensor(over[:, :, :], cnt[:, :].unsqueeze(2).to_broadcast([P, E, OVF]),
                                     C("thr").unsqueeze(1).to_broadcast([P, E, OVF]), ALU.is_gt))
                link(V.tensor_reduce(novf[:, :], over[:, :, :], AX.X, ALU.add))
                link(V.tensor_tensor(pre[:, :, :], C("tri").rearrange("p (a b) -> p a b", b=E),
                                     novf[:, :].unsqueeze(1).to_broadcast([P, E, E]), ALU.mult))
                link(V.tensor_reduce(incl[:, :], pre[:, :, :], AX.X, ALU.add))
                V.tensor_tensor(excl[:, :], incl[:, :], novf[:, :], ALU.subtract)
                link(V.tensor_tensor(tcmp[:, :, :], incl[:, :].unsqueeze(1).to_broadcast([P, OVF, E]),
                                     C("tilenum").unsqueeze(2).to_broadcast([P, OVF, E]), ALU.is_le))
                link(V.tensor_reduce(teid[:, 0:OVF], tcmp[:, :, :], AX.X, ALU.add))
                V.tensor_scalar(meta[:, 0:OVF], teid[:, 0:OVF], float(E - 1), None, ALU.min)
                link(V.tensor_copy(meta[:, OVF:OVF + 1], incl[:, E - 1:E]))
                link(V.tensor_tensor(rtmp[:, :, :], hot[:, :, :], over_j(excl[:, :]), ALU.mult))
                V.tensor_scalar(okey[:, 0, :], rank[:, :], float(P), -FAR, ALU.is_ge, ALU.mult)
                link(V.tensor_reduce(tbase[:, :], rtmp[:, :, :], AX.X, ALU.add))
                link(V.scalar_tensor_tensor(okey[:, 1, :], tbase[:, :], float(P), rank[:, :], ALU.mult, ALU.add))
                V.scalar_tensor_tensor(okey[:, 2, :], okey[:, 1, :], FAR - P, okey[:, 0, :], ALU.add, ALU.add)\
                    .then_inc(q["meta_ready"], 1)

            def rows_turned(t):
                dve.wait_ge(q["xt_ps"], t + 1)
                if t >= 2:
                    dve.wait_ge(q["hidden_ps"], 2 * (t - 1))
                V.tensor_copy(xt[:, t % 2, :, :],
                              ps[:, 6 + t % 2, 0:D].rearrange("p (k n) -> p k n", k=KD))\
                    .then_inc(q["xt_ready"], 1)

            def result(t):
                b2t = tile_of(t)[2]
                dve.wait_ge(q["y_ps"], t + 1)
                c = V.tensor_tensor(ysum[:, t % 2, :], ps[:, 4 + t % 2, 0:D], b2t, ALU.add)
                link(c)
                if t >= 2:
                    dve.wait_ge(scattered[t % 2], 16 * (t // 2))
                V.scalar_tensor_tensor(yout[:, t % 2, :], ysum[:, t % 2, :], slotscore[:, t:t + 1],
                                       rows[:, t % RING, 0:D], ALU.mult, ALU.add).then_inc(q["y_ready"], 1)

            dve.wait_ge(q["loaded_b2"], 16)
            rows_turned(0)
            rows_turned(1)
            overflow()
            for t in range(1, E):
                if t + 1 < E:
                    rows_turned(t + 1)
                result(t - 1)
            result(E - 1)
            dve.wait_ge(q["meta_ready"], 1)
            n = dve.value_load(meta[0:1, OVF:OVF + 1], min_val=0, max_val=OVF)
            with dve.If(n > 0):
                for j in range(NT):
                    m = V.tensor_scalar(place[:, j, 0:OVF * P], C("iota")[:, 0:OVF * P], okey[:, 2, j:j + 1], None,
                                        ALU.is_equal)
                m.then_inc(q["oplace_ready"], 1)
                dve.wait_ge(q["oinfo_ps"], 1)
                slots(E, E + OVF, q["oslots_ready"])
            for i in range(OVF):
                with dve.If(n > i):
                    rows_turned(E + i)
                    result(E + i)

        @block.gpsimd
        def _(pool):
            pool.memset(qt[:, :, T:TP], 0.0)
            pool.memset(ot[:, :, T:TP], 0.0)
            pool.memset(probs[:, :, HS:(HH + 1) * S], 0.0).then_inc(q["pads_ready"], 1)
            pool.wait_ge(q["loaded_cf"], 16)
            pool.wait_ge(q["wg_sq"], 1)
            pool.tensor_tensor(wgv[:, 1:2], wgv[:, 0:1], C("pow")[0:E, 1:2], ALU.pow).then_inc(q["wg_norm"], 1)
            for j in range(NT):
                pool.wait_ge(q["veps_ready"], j + 1)
                pool.tensor_tensor(rstd[:, j:j + 1], veps[:, j:j + 1], C("pow")[:, 0:1], ALU.pow)\
                    .then_inc(q["rstd_ready"], 1)
            pool.memset(vbd, 0.0).then_inc(q["v_zeroed"], 1)
            pool.wait_ge(q["v_zeroed"], 1)
            pool.tensor_copy(
                vbd[:, 0:B * VI].rearrange("p (a h w) -> p a h w", a=B // 2, w=VW)[:, :, :, DH],
                C("vmask")[0:GS, :].unsqueeze(1).to_broadcast([GS, B // 2, 2 * HEADS])).then_inc(q["v_zeroed"], 1)
            pool.wait_ge(q["loaded_bout"], 16)
            for j in range(NT):
                pool.wait_ge(q["xn_ready"], j + 1)
                pool.tensor_tensor(h[:, j, :], h[:, j, :], bout[:, :], ALU.add).then_inc(q["hb_ready"], 1)
            for j in range(NT):
                pool.wait_ge(q["veps2_ready"], j + 1)
                pool.tensor_tensor(rstd2[:, j:j + 1], veps2[:, j:j + 1], C("pow")[:, 0:1], ALU.pow)\
                    .then_inc(q["rstd2_ready"], 1)

            def gather(t):
                pool.indirect_dma_start(rows[:, t % RING, :], None, hz_d,
                                        bass.IndirectOffsetOnAxis(growu[:, t:t + 1], 0)).then_inc(gathered[t % RING], 16)

            def scatter(t):
                pool.wait_ge(q["y_ready"], t + 1)
                pool.indirect_dma_start(out, bass.IndirectOffsetOnAxis(srowu[:, t:t + 1], 0), yout[:, t % 2, :], None,
                                        bounds_check=T - 1, oob_is_err=False).then_inc(scattered[t % 2], 16)

            pool.wait_ge(q["hz_stored"], 16 * NT)
            for t in range(RING):
                pool.wait_ge(q["slots_ready"], 1 if t < 2 else 2)
                gather(t)
            for t in range(E):
                scatter(t)
                if t + RING < E:
                    gather(t + RING)
            pool.wait_ge(q["meta_ready"], 1)
            n = pool.value_load(meta[0:1, OVF:OVF + 1], min_val=0, max_val=OVF)
            with pool.If(n > 0):
                pool.wait_ge(q["oslots_ready"], 1)
                pool.nop()
            for i in range(OVF):
                with pool.If(n > i):
                    gather(E + i)
                    scatter(E + i)
                    pool.wait_ge(scattered[i % 2], 16 * ((E + i) // 2 + 1))


_OUT = ((B, S, D), "float32")


def kernel(**inputs):
    import concourse.bacc as _bacc
    from concourse.bass_utils import run_bass_kernel_spmd as _run

    a = {n: np.ascontiguousarray(v) for n, v in inputs.items()}
    x = a["x"].reshape(B, 6, 16, 6, 16, 3).transpose(2, 4, 5, 0, 1, 3).reshape(PD, B, PATCHES)
    emb = np.zeros((PD, TP + D), np.float32)
    emb[:, :T].reshape(PD, B, S)[:, :, 1:] = x
    emb[:, TP:] = a["L0_tok_W_proj"].T
    table = np.concatenate([a["cls_tok"].reshape(1, D), a["L0_tok_pos_emb"], a["L0_tok_b_proj"].reshape(1, D)])
    bqkv = a["L0_attn_b_qkv"].reshape(3 * KD, P)
    cf, cb, sel = constants()
    arrays = {
        "embed_in": emb.reshape(KE, P, TP + D),
        "table": table,
        "w_qkv": a["L0_attn_W_qkv"],
        "b_qk": bqkv[0:2 * KD].T,
        "b_v": bqkv[2 * KD:].T,
        "w_out": a["L0_attn_W_out"],
        "b_out": a["L0_attn_b_out"],
        "wg": a["L0_ffn_wg"],
        "w_red_t": a["L0_ffn_w_red"].T,
        "w1": a["L0_ffn_w1"],
        "b1": a["L0_ffn_b1"].reshape(E, FT, P).transpose(0, 2, 1),
        "w2": a["L0_ffn_w2"],
        "b2": a["L0_ffn_b2"],
        "const_f32": cf,
        "const_bf16": cb,
        "const_sel": sel,
    }
    arrays = {n: np.ascontiguousarray(v) for n, v in arrays.items()}
    nc = _bacc.Bacc("TRN2", target_bir_lowering=False, num_devices=1)
    args = [nc.dram_tensor(n, v.shape, mybir.dt.from_np(v.dtype), kind="ExternalInput").ap() for n, v in arrays.items()]
    out = nc.dram_tensor("out", [T, D], F32, kind="ExternalOutput").ap()
    vit_tower(nc, *args, out)
    r = _run(nc, [arrays], core_ids=[0])
    return r.results[0]["out"].reshape(_OUT[0])
```
